# Optimizing a Trainium2 kernel written in Bass

```python
import numpy as np
import jax
import jax.numpy as jnp

def _softmax(x, axis=-1):
    return jax.nn.softmax(x, axis=axis)

def _gelu(x):
    return jax.nn.gelu(x, approximate=True)

def _silu(x):
    return jax.nn.silu(x)

def _sigmoid(x):
    return jax.nn.sigmoid(x)

def _layernorm(x, axis=-1, eps=1e-05):
    m = jnp.mean(x, axis=axis, keepdims=True)
    v = jnp.var(x, axis=axis, keepdims=True)
    return (x - m) / jnp.sqrt(v + eps)

def _scatter_add(tgt, idx, src, axis=0):
    return tgt.at[idx].add(src)

def _segment_sum(src, seg, n):
    return jax.ops.segment_sum(src, seg, n)
kernel_name = 'mk_audio_tower_d1_tok_audfeat2048_r4_199ca7'

def setup_inputs(seed: int=0):
    np.random.seed(seed)
    _w = jnp.asarray

    def _rec_inputs():
        import jax
        import jax.numpy as jnp
        _rk = jax.random.key(seed)
        x = -0.000520686 + 1.00062 * jax.random.normal(jax.random.fold_in(_rk, 1), (64, 750, 1), jnp.float32)
        return x
    x = _rec_inputs()

    def _L0_tok_setup():
        import jax, jax.numpy as jnp
        import numpy as np
        PATCH_LEN = 128
        D_MODEL = 512
        BATCH = 128
        SEQ_LEN = 4096
        FEATURES = 1
        key = jax.random.key(seed)
        k1, k2, k3 = jax.random.split(key, 3)
        x = jax.random.normal(k1, (BATCH, SEQ_LEN, FEATURES), dtype=jnp.float32)
        W = jax.random.normal(k2, (D_MODEL, PATCH_LEN), dtype=jnp.float32) * (1.0 / np.sqrt(PATCH_LEN))
        b = jax.random.normal(k3, (D_MODEL,), dtype=jnp.float32) * 0.01
        return {'x': x, 'W': W, 'b': b}
    _L0_tok_all = _L0_tok_setup()
    _L0_tok_in = {k: v for k, v in _L0_tok_all.items() if k in ('W', 'b')}
    del _L0_tok_all

    def _L0_attn_setup():
        import jax, jax.numpy as jnp
        import numpy as np
        B_, L_ = (1, 256)
        D_MODEL, D_INNER, D_XB = (512, 1024, 256)
        D_STATE = 16
        DT_RANK = 128
        INTER = 2048
        EPS = 1e-05
        GC = D_INNER // D_STATE
        REP = D_INNER // D_XB

        def _rmsnorm(x, w):
            return x * jax.lax.rsqrt(jnp.mean(x * x, axis=-1, keepdims=True) + EPS) * w

        def _mamba(x, in_proj_w, dt_proj_w, dt_proj_b, A_log, D_skip, out_proj_w):
            b, l, _ = x.shape
            zxbcdt = x @ in_proj_w.T
            z = zxbcdt[..., :D_INNER]
            xv = zxbcdt[..., D_INNER:D_INNER + D_XB]
            Bm = zxbcdt[..., D_INNER + D_XB:D_INNER + 2 * D_XB]
            Cm = zxbcdt[..., D_INNER + 2 * D_XB:2 * D_INNER + 2 * D_XB]
            dt_in = zxbcdt[..., 2 * D_INNER + 2 * D_XB:]
            dt = jax.nn.softplus(dt_in @ dt_proj_w.T + dt_proj_b)
            xg = jnp.repeat(xv.reshape(b, l, D_XB // D_STATE, D_STATE), REP, axis=2)
            Bg = jnp.repeat(Bm.reshape(b, l, D_XB // D_STATE, D_STATE), REP, axis=2)
            Cg = Cm.reshape(b, l, GC, D_STATE)
            x_full = xg.reshape(b, l, D_INNER)
            A = -jnp.exp(A_log)
            dA = jnp.exp(dt[..., None] * A)
            dtx = (dt * x_full).reshape(b, l, GC, D_INNER // GC)
            dBx = (dtx[..., :, None] * Bg[..., None, :]).reshape(b, l, D_INNER, D_STATE)

            def step(h, inp):
                dA_i, dBx_i, C_i = inp
                h = dA_i * h + dBx_i
                y = jnp.einsum('bgn,bgcn->bgc', C_i, h.reshape(b, GC, D_INNER // GC, D_STATE))
                return (h, y.reshape(b, D_INNER))
            h0 = jnp.zeros((b, D_INNER, D_STATE), x.dtype)
            _, ys = jax.lax.scan(step, h0, (dA.transpose(1, 0, 2, 3), dBx.transpose(1, 0, 2, 3), Cg.transpose(1, 0, 2, 3)))
            y = ys.transpose(1, 0, 2) + D_skip * x_full
            y = y * jax.nn.silu(z)
            return y @ out_proj_w.T
        key = jax.random.key(seed)
        ks = jax.random.split(key, 8)
        s = 0.02
        return {'hidden_states': jax.random.normal(ks[0], (B_, L_, D_MODEL), jnp.float32), 'rms1_w': jnp.ones((D_MODEL,), jnp.float32), 'in_proj_w': jax.random.normal(ks[1], (2 * D_INNER + 2 * D_XB + DT_RANK, D_MODEL), jnp.float32) * s, 'dt_proj_w': jax.random.normal(ks[2], (D_INNER, DT_RANK), jnp.float32) * s, 'dt_proj_b': jax.random.normal(ks[3], (D_INNER,), jnp.float32) * 0.5 - 4.0, 'A_log': jnp.tile(jnp.log(jnp.arange(1, D_STATE + 1, dtype=jnp.float32)), (D_INNER, 1)), 'D_skip': jnp.ones((D_INNER,), jnp.float32), 'out_proj_w': jax.random.normal(ks[4], (D_MODEL, D_INNER), jnp.float32) * s, 'rms2_w': jnp.ones((D_MODEL,), jnp.float32), 'gate_w': jax.random.normal(ks[5], (INTER, D_MODEL), jnp.float32) * s, 'up_w': jax.random.normal(ks[6], (INTER, D_MODEL), jnp.float32) * s, 'down_w': jax.random.normal(ks[7], (D_MODEL, INTER), jnp.float32) * s}
    _L0_attn_all = _L0_attn_setup()
    _L0_attn_in = {k: v for k, v in _L0_attn_all.items() if k in ('rms1_w', 'in_proj_w', 'dt_proj_w', 'dt_proj_b', 'A_log', 'D_skip', 'out_proj_w', 'rms2_w', 'gate_w', 'up_w', 'down_w')}
    del _L0_attn_all

    def _L0_ffn_setup():
        import jax, jax.numpy as jnp
        import numpy as np
        DIM_IN = 512
        DIM_HIDDEN = 2048
        key = jax.random.key(seed)
        k_x, k_g, k_u, k_d = jax.random.split(key, 4)
        s_in = 1.0 / np.sqrt(DIM_IN)
        s_hid = 1.0 / np.sqrt(DIM_HIDDEN)
        x = jax.random.normal(k_x, (4, 512, DIM_IN), dtype=jnp.float32)
        w_gate = jax.random.uniform(k_g, (DIM_HIDDEN, DIM_IN), jnp.float32, -s_in, s_in)
        w_up = jax.random.uniform(k_u, (DIM_HIDDEN, DIM_IN), jnp.float32, -s_in, s_in)
        w_down = jax.random.uniform(k_d, (DIM_IN, DIM_HIDDEN), jnp.float32, -s_hid, s_hid)
        return {'x': x, 'w_gate': w_gate, 'w_up': w_up, 'w_down': w_down}
    _L0_ffn_all = _L0_ffn_setup()
    _L0_ffn_in = {k: v for k, v in _L0_ffn_all.items() if k in ('w_gate', 'w_up', 'w_down')}
    del _L0_ffn_all
    return {'x': x, 'L0_tok_W': _L0_tok_in['W'], 'L0_tok_b': _L0_tok_in['b'], 'L0_attn_rms1_w': _L0_attn_in['rms1_w'], 'L0_attn_in_proj_w': _L0_attn_in['in_proj_w'], 'L0_attn_dt_proj_w': _L0_attn_in['dt_proj_w'], 'L0_attn_dt_proj_b': _L0_attn_in['dt_proj_b'], 'L0_attn_A_log': _L0_attn_in['A_log'], 'L0_attn_D_skip': _L0_attn_in['D_skip'], 'L0_attn_out_proj_w': _L0_attn_in['out_proj_w'], 'L0_attn_rms2_w': _L0_attn_in['rms2_w'], 'L0_attn_gate_w': _L0_attn_in['gate_w'], 'L0_attn_up_w': _L0_attn_in['up_w'], 'L0_attn_down_w': _L0_attn_in['down_w'], 'L0_ffn_w_gate': _L0_ffn_in['w_gate'], 'L0_ffn_w_up': _L0_ffn_in['w_up'], 'L0_ffn_w_down': _L0_ffn_in['w_down']}

def reference(x, L0_tok_W, L0_tok_b, L0_attn_rms1_w, L0_attn_in_proj_w, L0_attn_dt_proj_w, L0_attn_dt_proj_b, L0_attn_A_log, L0_attn_D_skip, L0_attn_out_proj_w, L0_attn_rms2_w, L0_attn_gate_w, L0_attn_up_w, L0_attn_down_w, L0_ffn_w_gate, L0_ffn_w_up, L0_ffn_w_down):
    import jax
    import jax.numpy as jnp

    def _L0_tok_ref(x, W, b):
        import jax, jax.numpy as jnp
        import numpy as np
        PATCH_LEN = 128
        D_MODEL = 512
        BATCH = 128
        SEQ_LEN = 4096
        FEATURES = 1
        B, S, F = x.shape
        P = PATCH_LEN
        stride = P // 2
        starts = jnp.arange(0, S - P + 1, stride)
        idx = starts[:, None] + jnp.arange(P)
        patches = x[:, idx, :].reshape(B, starts.shape[0], P * F)
        patches = patches[:, :, :P]
        return jnp.einsum('bnp,dp->bnd', patches, W) + b

    def _L0_attn_ref(hidden_states, rms1_w, in_proj_w, dt_proj_w, dt_proj_b, A_log, D_skip, out_proj_w, rms2_w, gate_w, up_w, down_w):
        import jax, jax.numpy as jnp
        import numpy as np
        B_, L_ = (1, 256)
        D_MODEL, D_INNER, D_XB = (512, 1024, 256)
        D_STATE = 16
        DT_RANK = 128
        INTER = 2048
        EPS = 1e-05
        GC = D_INNER // D_STATE
        REP = D_INNER // D_XB

        def _rmsnorm(x, w):
            return x * jax.lax.rsqrt(jnp.mean(x * x, axis=-1, keepdims=True) + EPS) * w

        def _mamba(x, in_proj_w, dt_proj_w, dt_proj_b, A_log, D_skip, out_proj_w):
            b, l, _ = x.shape
            zxbcdt = x @ in_proj_w.T
            z = zxbcdt[..., :D_INNER]
            xv = zxbcdt[..., D_INNER:D_INNER + D_XB]
            Bm = zxbcdt[..., D_INNER + D_XB:D_INNER + 2 * D_XB]
            Cm = zxbcdt[..., D_INNER + 2 * D_XB:2 * D_INNER + 2 * D_XB]
            dt_in = zxbcdt[..., 2 * D_INNER + 2 * D_XB:]
            dt = jax.nn.softplus(dt_in @ dt_proj_w.T + dt_proj_b)
            xg = jnp.repeat(xv.reshape(b, l, D_XB // D_STATE, D_STATE), REP, axis=2)
            Bg = jnp.repeat(Bm.reshape(b, l, D_XB // D_STATE, D_STATE), REP, axis=2)
            Cg = Cm.reshape(b, l, GC, D_STATE)
            x_full = xg.reshape(b, l, D_INNER)
            A = -jnp.exp(A_log)
            dA = jnp.exp(dt[..., None] * A)
            dtx = (dt * x_full).reshape(b, l, GC, D_INNER // GC)
            dBx = (dtx[..., :, None] * Bg[..., None, :]).reshape(b, l, D_INNER, D_STATE)

            def step(h, inp):
                dA_i, dBx_i, C_i = inp
                h = dA_i * h + dBx_i
                y = jnp.einsum('bgn,bgcn->bgc', C_i, h.reshape(b, GC, D_INNER // GC, D_STATE))
                return (h, y.reshape(b, D_INNER))
            h0 = jnp.zeros((b, D_INNER, D_STATE), x.dtype)
            _, ys = jax.lax.scan(step, h0, (dA.transpose(1, 0, 2, 3), dBx.transpose(1, 0, 2, 3), Cg.transpose(1, 0, 2, 3)))
            y = ys.transpose(1, 0, 2) + D_skip * x_full
            y = y * jax.nn.silu(z)
            return y @ out_proj_w.T
        res = hidden_states
        h = _rmsnorm(hidden_states, rms1_w)
        h = res + _mamba(h, in_proj_w, dt_proj_w, dt_proj_b, A_log, D_skip, out_proj_w)
        res = h
        hn = _rmsnorm(h, rms2_w)
        mlp = jax.nn.silu(hn @ gate_w.T) * (hn @ up_w.T) @ down_w.T
        return res + mlp

    def _L0_ffn_ref(x, w_gate, w_up, w_down):
        import jax, jax.numpy as jnp
        import numpy as np
        DIM_IN = 512
        DIM_HIDDEN = 2048
        gate = jnp.einsum('bsd,hd->bsh', x, w_gate)
        up = jnp.einsum('bsd,hd->bsh', x, w_up)
        gated = jax.nn.silu(gate) * up
        return jnp.einsum('bsh,dh->bsd', gated, w_down)
    h = _L0_tok_ref(x, L0_tok_W, L0_tok_b)
    h = h + _L0_attn_ref(_layernorm(h, axis=-1), L0_attn_rms1_w, L0_attn_in_proj_w, L0_attn_dt_proj_w, L0_attn_dt_proj_b, L0_attn_A_log, L0_attn_D_skip, L0_attn_out_proj_w, L0_attn_rms2_w, L0_attn_gate_w, L0_attn_up_w, L0_attn_down_w)
    h = h + _L0_ffn_ref(_layernorm(h, axis=-1), L0_ffn_w_gate, L0_ffn_w_up, L0_ffn_w_down)
    return h

_drawn_inputs = setup_inputs


def setup_inputs(seed=0):
    import zlib

    import numpy as np

    out = dict(_drawn_inputs(seed))
    spreads = {'L0_attn_rms1_w': (1.0, 0.6), 'L0_attn_D_skip': (1.0, 0.6), 'L0_attn_rms2_w': (1.0, 0.6)}
    factors = {'L0_tok_b': 5.646,
     'L0_attn_dt_proj_w': 8.0,
     'L0_attn_dt_proj_b': 8.0,
     'L0_attn_A_log': 8.0}
    for name, (base, spread) in spreads.items():
        noise = np.random.default_rng([zlib.crc32(name.encode()), seed]).standard_normal(out[name].shape)
        drawn = base * np.exp(spread * noise) if base else spread * noise
        out[name] = jnp.asarray(drawn.astype(out[name].dtype))
    for name, factor in factors.items():
        out[name] = (out[name] * factor).astype(out[name].dtype)
    return out
```

```python
from contextlib import ExitStack

import concourse.bass as bass
from concourse import mybir

F32 = mybir.dt.float32
ALU = mybir.AluOpType
ACT = mybir.ActivationFunctionType

P = 128
BATCH, SERIES = 64, 750
PATCH, HOP = 128, 64
STEPS = (SERIES // HOP) - 1
D = 512
DI = 1024
XB = 256
NS = 16
HID = 2048
EPS = 1e-5

NCH = 2
CB = BATCH // NCH
T = CB * STEPS
KD = D // P
KI = DI // P
HT = HID // P
NQ = 4
QU = NS // NQ
UNITS = KI * QU
BANK = 512

IN_DT, IN_X, IN_B, IN_CZ = 0, 1, 3, 5
IN_TILES = 5 + 2 * KI
IN_GROUPS = [(0, 5), (5, 9), (9, 13), (13, 17), (17, 21)]

S_TOKB, S_DTB, S_DSKIP, S_W1, S_W2 = 0, 4, 12, 20, 24
S_ALOG = 28
S_PICKX = S_ALOG + KI * NS
S_PICKC = S_PICKX + P
S_COLS = S_PICKC + NQ * P

NH, NB, ND, NG = 3, 3, 2, 4
WSLOT = 1024
MLP_LOADS = HT + 2 * KD


def a_steps(c):
    head = [("tok", c), ("ln1_mean", c), ("ln1_var", c), ("rms1", c), ("in_dt", c), ("in_x", c, 0), ("in_x", c, 1),
            ("in_b", c, 0), ("in_b", c, 1)]
    tiles = [[("dtp", c, m), ("xs", c, m), ("in_c", c, m), ("in_z", c, m)] for m in range(KI)]
    return head, tiles


def m_steps(c):
    s = [("out", c, o) for o in range(KD)] + [("rms2", c)]
    s += [("gu", c, 0, j) for j in range(HT)] + [("down", c, 0, o) for o in range(KD)]
    s += [("ln2_mean", c), ("ln2_var", c)]
    s += [("gu", c, 1, j) for j in range(HT)] + [("down", c, 1, o) for o in range(KD)]
    return s


def schedule():
    head0, tiles0 = a_steps(0)
    head1, tiles1 = a_steps(1)
    slots = [(None, head0 + [s for t in tiles0 for s in t])]
    for u in range(UNITS):
        if u < 4:
            bg = [head1[0:2], head1[2:3], head1[3:4], head1[4:9]][u]
        else:
            bg = [tiles1[u // 4 - 1][u % 4]]
        slots.append((u, bg))
    steps = m_steps(0)
    first = [tiles1[KI - 1] + steps[0:1], steps[1:3], steps[3:4]]
    rest, left = steps[4:], UNITS - len(first)
    for u, bg in enumerate(first):
        slots.append((UNITS + u, bg))
    for u in range(left):
        slots.append((UNITS + len(first) + u, rest[len(rest) * u // left:len(rest) * (u + 1) // left]))
    slots.append((None, m_steps(1)))
    return slots


def work_bank_uses():
    uses = {}
    for _, steps in schedule():
        for s in steps:
            names = {"tok": [("tok", s[1], k) for k in range(KD)],
                     "gu": [(s, "gate"), (s, "up")]}.get(s[0], [s])
            for n in names:
                uses[n] = len(uses)
    return uses


def build(nc, patches, tok_w, small, w_in, w_dt, w_out, w_mlp, out):
    slots = schedule()
    uses = work_bank_uses()
    silus = {s: i for i, s in enumerate(s for _, steps in slots for s in steps if s[0] in ("in_z", "gu"))}
    b_dram = nc.dram_tensor("b_rows", (NCH, XB, T), F32, kind="Internal").ap()

    with ExitStack() as ctx:
        def sb(name, shape):
            return ctx.enter_context(nc.sbuf_tensor(name, shape, F32))

        def sem(name):
            return ctx.enter_context(nc.semaphore(name))

        pat = sb("pat", [P, NCH, T])
        tokw = sb("tokw", [P, D])
        sm = sb("sm", [P, S_COLS])
        a_neg = sb("a_neg", [P, KI * NS])
        mean_w = sb("mean_w", [P, P])
        shared = sb("shared", [P, IN_TILES * D + DI])
        win = shared[:, 0:IN_TILES * D].rearrange("p (t f) -> p t f", f=D)
        wdt = shared[:, IN_TILES * D:]
        NW = (IN_TILES * D + DI - HT * T) // WSLOT
        gated = shared[:, 0:HT * T].rearrange("p (j t) -> p j t", t=T)
        wring = shared[:, HT * T:HT * T + NW * WSLOT].rearrange("p (s f) -> p s f", f=WSLOT)
        wout = sb("wout", [P, KI, D])
        h = sb("h", [P, NCH, KD, T])
        a = sb("a", [P, NCH, KD, T])
        sq = sb("sq", [P, KD, T])
        xv = sq[:, 0:2, :]
        bs = sq[:, 2:4, :]
        hn = sb("hn", [P, KD, T])
        rstd_ln = sb("rstd_ln", [P, T])
        rstd = sb("rstd", [P, T])
        dti = sb("dti", [P, T])
        dt = sb("dt", [P, KI, T])
        xf = sb("xf", [P, KI, T])
        cm = sb("cm", [P, KI, T])
        z = sb("z", [P, KI, T])
        yg = sb("yg", [P, KI, T])
        sp_u = sb("sp_u", [P, T])
        sp_l = sb("sp_l", [P, T])
        sp_e = sb("sp_e", [P, T])
        th = sb("th", [P, 2, T])
        gs = sp_e
        dtx = sb("dtx", [P, 2, T])
        bb = sb("bb", [P, NB, NQ * T])
        da = sb("da", [P, ND, NQ * T])
        hs = sb("hs", [P, NH, NQ, T])
        acc = sb("acc", [P, 2, T])
        ysum = sb("ysum", [P, T])
        eps_col = sb("eps_col", [P, 1])
        eps_ap = eps_col[:, :]

        work = [ctx.enter_context(nc.psum_tensor(f"work{i}", [P, BANK], F32)) for i in range(NG)]
        cps = [ctx.enter_context(nc.psum_tensor(f"c_bcast{i}", [P, 2, BANK], F32)) for i in range(2)]

        pat_loaded, tokw_loaded, small_loaded = sem("pat_loaded"), sem("tokw_loaded"), sem("small_loaded")
        win_loaded = [sem(f"win_loaded{g}") for g in range(len(IN_GROUPS))]
        wdt_loaded, wout_loaded = sem("wdt_loaded"), sem("wout_loaded")
        w_loaded = [sem(f"w_loaded{i}") for i in range(NW)]
        bb_loaded = [sem(f"bb_loaded{i}") for i in range(NB)]
        b_stored = sem("b_stored")
        out_stored = sem("out_stored")
        consts_done = sem("consts_done")
        a_neg_exp = sem("a_neg_exp")
        a_neg_done = sem("a_neg_done")
        bank_full = [sem(f"bank_full{i}") for i in range(NG)]
        bank_free = [sem(f"bank_free{i}") for i in range(NG)]
        h_done = sem("h_done")
        centered = sem("centered")
        sq_done = sem("sq_done")
        ln_done = sem("ln_done")
        rstd_done = sem("rstd_done")
        norm_done = sem("norm_done")
        dti_done, xv_done, bs_done = sem("dti_done"), sem("xv_done"), sem("bs_done")
        sp_act = sem("sp_act")
        dt_ready, x_ready, c_ready, z_ready = sem("dt_ready"), sem("x_ready"), sem("c_ready"), sem("z_ready")
        th_done, th_used = sem("th_done"), sem("th_used")
        dtx_done, dbx_done, da_done, da_zeroed = sem("dtx_done"), sem("dbx_done"), sem("da_done"), sem("da_zeroed")
        scan_done, h_used, y_done = sem("scan_done"), sem("h_used"), sem("y_done")
        c_full, c_free = sem("c_full"), sem("c_free")
        res_done = sem("res_done")
        gated_done = sem("gated_done")
        h1_done, final_done = sem("h1_done"), sem("final_done")
        dve_chain = sem("dve_chain")

        def bank(name):
            return work[uses[name] % NG][:, 0:T]

        def full(eng, name):
            name = (name, "up") if name[0] == "gu" else name
            eng.wait_ge(bank_full[uses[name] % NG], uses[name] // NG + 1)

        def free_of(name):
            return bank_free[uses[name] % NG]

        def small_ap(col, i):
            return sm[:, col + i:col + i + 1]

        def norm_index(name, c):
            return [("ln1", 0), ("rms1", 0), ("ln1", 1), ("rms1", 1), ("rms2", 0), ("ln2", 0), ("rms2", 1),
                    ("ln2", 1)].index((name, c))

        def ln_index(name, c):
            return [("ln1", 0), ("ln1", 1), ("ln2", 0), ("ln2", 1)].index((name, c))

        def load_index(c, mlp, i):
            return (2 * c + mlp) * MLP_LOADS + i

        block = ctx.enter_context(nc.Block())

        @block.sync
        def _(sp):
            sp.dma_start(pat[:, :, :], patches).then_inc(pat_loaded, 16)
            sp.dma_start(tokw[:, :], tok_w).then_inc(tokw_loaded, 16)
            sp.dma_start(sm[:, :], small).then_inc(small_loaded, 16)
            for g, (lo, hi) in enumerate(IN_GROUPS):
                sp.dma_start(win[:, lo:hi, :], w_in[:, lo:hi, :]).then_inc(win_loaded[g], 16)
                if g == 0:
                    sp.dma_start(wdt, w_dt).then_inc(wdt_loaded, 16)
            sp.dma_start(wout[:, :, :], w_out).then_inc(wout_loaded, 16)

            def load_b(u):
                c, m, q = u // UNITS, u % UNITS // QU, u % QU
                if u >= NB:
                    sp.wait_ge(dbx_done, u - NB + 1)
                if u % UNITS == 0:
                    sp.wait_ge(b_stored, 16 * (c + 1))
                rows = b_dram[c].rearrange("(g n) t -> g (n t)", n=NS)
                for g in range(2):
                    src = rows[2 * m + g:2 * m + g + 1, q * NQ * T:(q + 1) * NQ * T].to_broadcast([64, NQ * T])
                    sp.dma_start(bb[64 * g:64 * g + 64, u % NB, :], src).then_inc(bb_loaded[u % NB], 16)

            def last_reader(i):
                c, mlp, k = i // (2 * MLP_LOADS), i // MLP_LOADS % 2, i % MLP_LOADS
                return ("gu", c, mlp, k) if k < HT else ("down", c, mlp, (k - HT) // 2)

            def load_w(i):
                if i == 0:
                    full(sp, ("in_z", 1, KI - 1))
                if i >= NW:
                    full(sp, last_reader(i - NW))
                sp.dma_start(wring[:, i % NW, :], w_mlp[i % (2 * MLP_LOADS)]).then_inc(w_loaded[i % NW], 16)

            for unit, steps in slots:
                if unit is not None:
                    load_b(unit)
                for s in steps:
                    if s[0] == "in_b" and s[2] == 1:
                        sp.wait_ge(bs_done, 2 * (s[1] + 1))
                        sp.dma_start(b_dram[s[1]].rearrange("(i p) t -> p i t", p=P), bs[:, :, :]).then_inc(b_stored, 16)
                    if s[0] == "gu":
                        load_w(load_index(s[1], s[2], s[3]))
                    if s[0] == "down":
                        for half in range(2):
                            load_w(load_index(s[1], s[2], HT + 2 * s[3] + half))
                        if s[2] == 1:
                            sp.wait_ge(final_done, KD * s[1] + s[3] + 1)
                            sp.dma_start(out[s[3] * P:(s[3] + 1) * P, s[1] * T:(s[1] + 1) * T],
                                         h[:, s[1], s[3], :]).then_inc(out_stored, 16)
            sp.wait_ge(out_stored, 16 * NCH * KD)

        @block.gpsimd
        def _(pool):
            nc.gpsimd.memset(da[:, :, :], 0.0).then_inc(da_zeroed, 1)
            for u in range(NCH * UNITS):
                c, m, q = u // UNITS, u % UNITS // QU, u % QU
                t = c * KI + m
                if q == 0:
                    pool.wait_ge(dt_ready, t + 1)
                    pool.wait_ge(x_ready, t + 1)
                    if t >= 2:
                        pool.wait_ge(dbx_done, QU * (t - 1))
                    nc.gpsimd.tensor_tensor(dtx[:, t % 2, :], dt[:, m, :], xf[:, m, :], ALU.mult).then_inc(dtx_done, 1)
                    pool.wait_ge(dtx_done, t + 1)
                pool.wait_ge(bb_loaded[u % NB], 32 * (u // NB + 1))
                if u >= NH:
                    pool.wait_ge(h_used, u - NH + 1)
                nc.gpsimd.tensor_tensor(hs[:, u % NH, :, :], dtx[:, t % 2, :].unsqueeze(1).to_broadcast([P, NQ, T]),
                                        bb[:, u % NB, :].rearrange("p (n t) -> p n t", t=T),
                                        ALU.mult).then_inc(dbx_done, 1)

        @block.scalar
        def _(act):
            act.wait_ge(small_loaded, 16)
            nc.scalar.activation(a_neg[:, :], sm[:, S_ALOG:S_ALOG + KI * NS], ACT.Exp).then_inc(a_neg_exp, 1)

            def decay(u):
                c, m, q = u // UNITS, u % UNITS // QU, u % QU
                if u == 0:
                    act.wait_ge(da_zeroed, 1)
                    act.wait_ge(a_neg_done, 1)
                act.wait_ge(dt_ready, c * KI + m + 1)
                if u >= ND:
                    act.wait_ge(scan_done, u - ND + 1)
                src = dt[:, m, :].rearrange("p (b t) -> p b t", t=STEPS)[:, :, 1:]
                for i in range(NQ):
                    dst = da[:, u % ND, i * T:(i + 1) * T].rearrange("p (b t) -> p b t", t=STEPS)[:, :, 1:]
                    n = m * NS + q * NQ + i
                    last = nc.scalar.activation(dst, src, ACT.Exp, scale=a_neg[:, n:n + 1])
                last.then_inc(da_done, 1)

            def squares(x, v):
                stored = {2: 1, 4: 2}.get(v, 0)
                if stored:
                    act.wait_ge(b_stored, 16 * stored)
                nc.scalar.activation(sq[:, :, :], x, ACT.Square).then_inc(sq_done, 1)

            def inverse_root(name, v):
                full(act, name)
                nc.scalar.activation(rstd_ln[:, :], bank(name), ACT.Ln, bias=eps_ap).then_inc(free_of(name), 1)
                act.wait_ge(free_of(name), uses[name] // NG + 1)
                if v >= 1:
                    act.wait_ge(norm_done, v)
                nc.scalar.activation(rstd[:, :], rstd_ln[:, :], ACT.Exp, scale=-0.5).then_inc(rstd_done, 1)

            def step(s):
                kind, c = s[0], s[1]
                if kind == "tok":
                    for k in range(KD):
                        full(act, ("tok", c, k))
                        nc.scalar.activation(h[:, c, k, :], bank(("tok", c, k)), ACT.Identity,
                                             bias=small_ap(S_TOKB, k)).then_inc(free_of(("tok", c, k)), 1)
                        act.wait_ge(free_of(("tok", c, k)), uses[("tok", c, k)] // NG + 1)
                        act.sem_inc(h_done, 1)
                elif kind == "ln1_var":
                    act.wait_ge(centered, ln_index("ln1", c) + 1)
                    squares(a[:, c, :, :], norm_index("ln1", c))
                    inverse_root(s, norm_index("ln1", c))
                elif kind == "rms1":
                    act.wait_ge(norm_done, norm_index("ln1", c) + 1)
                    squares(a[:, c, :, :], norm_index("rms1", c))
                    inverse_root(s, norm_index("rms1", c))
                elif kind == "rms2":
                    act.wait_ge(res_done, KD * (c + 1))
                    squares(a[:, c, :, :], norm_index("rms2", c))
                    inverse_root(s, norm_index("rms2", c))
                elif kind == "ln2_var":
                    act.wait_ge(centered, ln_index("ln2", c) + 1)
                    squares(hn[:, :, :], norm_index("ln2", c))
                    inverse_root(s, norm_index("ln2", c))
                elif kind in ("in_dt", "in_x", "in_b", "xs", "in_c"):
                    dst, done = {"in_dt": lambda: (dti[:, :], dti_done), "in_x": lambda: (xv[:, s[2], :], xv_done),
                                 "in_b": lambda: (bs[:, s[2], :], bs_done), "xs": lambda: (xf[:, s[2], :], x_ready),
                                 "in_c": lambda: (cm[:, s[2], :], c_ready)}[kind]()
                    if kind in ("xs", "in_c") and c >= 1:
                        act.wait_ge(y_done, KI * (c - 1) + s[2] + 1)
                    full(act, s)
                    nc.scalar.copy(dst, bank(s)).then_inc(done, 1)
                    act.wait_ge(done, {"in_dt": c + 1, "in_x": 2 * c + s[-1] + 1, "in_b": 2 * c + s[-1] + 1}.get(
                        kind, KI * c + s[-1] + 1))
                    act.sem_inc(free_of(s), 1)
                elif kind == "in_z":
                    silu(s, s)
                elif kind == "dtp":
                    m = s[2]
                    i = KI * c + m
                    if c >= 1:
                        act.wait_ge(y_done, KI * (c - 1) + m + 1)
                    if i >= 1:
                        act.wait_ge(dt_ready, i)
                    full(act, s)
                    nc.scalar.activation(dt[:, m, :], bank(s), ACT.Identity, bias=small_ap(S_DTB, m))
                    nc.scalar.activation(sp_u[:, :], bank(s), ACT.Abs, bias=small_ap(S_DTB, m)).then_inc(free_of(s), 1)
                    act.wait_ge(free_of(s), uses[s] // NG + 1)
                    nc.scalar.activation(sp_u[:, :], sp_u[:, :], ACT.Exp, scale=-1.0).then_inc(sp_act, 1)
                    act.wait_ge(sp_act, 2 * i + 1)
                    nc.scalar.activation(sp_l[:, :], sp_u[:, :], ACT.Ln, bias=1.0).then_inc(sp_act, 1)
                elif kind == "gu":
                    silu(s, (s, "gate"))

            def silu(s, name):
                i = silus[s]
                full(act, name)
                if i >= 2:
                    act.wait_ge(th_used, i - 1)
                nc.scalar.activation(th[:, i % 2, :], bank(name), ACT.Tanh, scale=0.5).then_inc(th_done, 1)

            for i, (unit, steps) in enumerate(slots):
                if unit == 0:
                    decay(0)
                if unit is not None and unit + 1 < NCH * UNITS:
                    decay(unit + 1)
                for s in steps:
                    step(s)

        @block.vector
        def _(dve):
            chain = [0]

            def link(ins):
                chain[0] += 1
                ins.then_inc(dve_chain, 1)
                dve.wait_ge(dve_chain, chain[0])

            nc.vector.memset(eps_ap, EPS)
            nc.vector.memset(mean_w[:, :], 1.0 / D).then_inc(consts_done, 1)
            dve.wait_ge(a_neg_exp, 1)
            nc.vector.tensor_scalar(a_neg[:, :], a_neg[:, :], -1.0, None, ALU.mult).then_inc(a_neg_done, 1)

            def scan(u):
                c, m, q = u // UNITS, u % UNITS // QU, u % QU
                slot = hs[:, u % NH, :, :]
                flat = slot.rearrange("p n t -> p (n t)")
                dve.wait_ge(dbx_done, u + 1)
                dve.wait_ge(da_done, u + 1)
                nc.vector.tensor_tensor_scan(flat, da[:, u % ND, :], flat, 0.0, ALU.mult, ALU.add).then_inc(scan_done, 1)
                dve.wait_ge(scan_done, u + 1)
                for half in range(2):
                    pair = slot[:, 2 * half:2 * half + 2, :]
                    dve.wait_ge(c_full, 2 * u + half + 1)
                    nc.vector.tensor_tensor(pair, pair, cps[half][:, :, 0:T], ALU.mult).then_inc(c_free, 1)
                dve.wait_ge(c_free, 2 * u + 2)
                if q == 0:
                    nc.vector.tensor_tensor(acc[:, :, :], slot[:, 0:2, :], slot[:, 2:4, :], ALU.add).then_inc(h_used, 1)
                else:
                    link(nc.vector.tensor_tensor(acc[:, :, :], acc[:, :, :], slot[:, 0:2, :], ALU.add))
                    nc.vector.tensor_tensor(acc[:, :, :], acc[:, :, :], slot[:, 2:4, :], ALU.add).then_inc(h_used, 1)
                dve.wait_ge(h_used, u + 1)
                if q == QU - 1:
                    link(nc.vector.tensor_tensor(ysum[:, :], acc[:, 0, :], acc[:, 1, :], ALU.add))
                    dve.wait_ge(x_ready, KI * c + m + 1)
                    link(nc.vector.scalar_tensor_tensor(out=ysum[:, :], in0=xf[:, m, :], scalar=small_ap(S_DSKIP, m),
                                                        in1=ysum[:, :], op0=ALU.mult, op1=ALU.add))
                    dve.wait_ge(z_ready, KI * c + m + 1)
                    if c >= 1:
                        full(dve, ("out", c - 1, KD - 1))
                    nc.vector.scalar_tensor_tensor(out=yg[:, m, :], in0=ysum[:, :], scalar=0.5, in1=z[:, m, :],
                                                   op0=ALU.mult, op1=ALU.mult).then_inc(y_done, 1)

            def center(name, src, dst, done):
                full(dve, name)
                nc.vector.tensor_tensor(dst, src, bank(name).unsqueeze(1).to_broadcast([P, KD, T]),
                                        ALU.subtract).then_inc(centered, 1)
                dve.wait_ge(centered, done)
                dve.sem_inc(free_of(name), 1)

            def silu2(s, name, dst, done):
                i = silus[s]
                dve.wait_ge(th_done, i + 1)
                return nc.vector.scalar_tensor_tensor(out=dst, in0=th[:, i % 2, :], scalar=1.0, in1=bank(name),
                                                      op0=ALU.add, op1=ALU.mult)

            def step(s):
                kind, c = s[0], s[1]
                if kind == "ln1_mean":
                    center(s, h[:, c, :, :], a[:, c, :, :], ln_index("ln1", c) + 1)
                elif kind == "ln2_mean":
                    full(dve, ("gu", c, 0, HT - 1))
                    center(s, h[:, c, :, :], hn[:, :, :], ln_index("ln2", c) + 1)
                elif kind in ("ln1_var", "ln2_var"):
                    name = kind[0:3]
                    x = a[:, c, :, :] if name == "ln1" else hn[:, :, :]
                    dve.wait_ge(rstd_done, norm_index(name, c) + 1)
                    nc.vector.tensor_tensor(x, x, rstd[:, :].unsqueeze(1).to_broadcast([P, KD, T]),
                                            ALU.mult).then_inc(norm_done, 1)
                elif kind in ("rms1", "rms2"):
                    dve.wait_ge(rstd_done, norm_index(kind, c) + 1)
                    if (kind, c) != ("rms1", 0):
                        full(dve, {("rms1", 1): ("in_z", 0, KI - 1), ("rms2", 0): ("in_z", 1, KI - 1),
                                   ("rms2", 1): ("gu", 0, 1, HT - 1)}[kind, c])
                    for k in range(KD):
                        last = nc.vector.scalar_tensor_tensor(
                            out=hn[:, k, :], in0=a[:, c, k, :], scalar=small_ap(S_W1 if kind == "rms1" else S_W2, k),
                            in1=rstd[:, :], op0=ALU.mult, op1=ALU.mult)
                    last.then_inc(norm_done, 1)
                elif kind == "in_z":
                    if c >= 1:
                        dve.wait_ge(y_done, KI * (c - 1) + s[2] + 1)
                    silu2(s, s, z[:, s[2], :], None).then_inc(z_ready, 1)
                    dve.wait_ge(z_ready, KI * c + s[2] + 1)
                    dve.sem_inc(free_of(s), 1)
                    dve.sem_inc(th_used, 1)
                elif kind == "dtp":
                    i = KI * c + s[2]
                    dve.wait_ge(sp_act, 2 * i + 2)
                    link(nc.vector.tensor_scalar(sp_e[:, :], sp_u[:, :], 1.0, -1.0, ALU.add, ALU.add))
                    link(nc.vector.tensor_tensor(sp_u[:, :], sp_u[:, :], sp_e[:, :], ALU.subtract))
                    link(nc.vector.tensor_tensor(sp_u[:, :], sp_u[:, :], sp_l[:, :], ALU.add))
                    nc.vector.scalar_tensor_tensor(out=dt[:, s[2], :], in0=dt[:, s[2], :], scalar=0.0, in1=sp_u[:, :],
                                                   op0=ALU.max, op1=ALU.add).then_inc(dt_ready, 1)
                elif kind == "out":
                    full(dve, s)
                    nc.vector.tensor_tensor(a[:, c, s[2], :], a[:, c, s[2], :], bank(s), ALU.add).then_inc(res_done, 1)
                    dve.wait_ge(res_done, KD * c + s[2] + 1)
                    dve.sem_inc(free_of(s), 1)
                elif kind == "gu":
                    mlp, j = s[2], s[3]
                    link(silu2(s, (s, "gate"), gs[:, :], None))
                    dve.sem_inc(free_of((s, "gate")), 1)
                    dve.sem_inc(th_used, 1)
                    full(dve, (s, "up"))
                    if j == 0 and c + mlp == 0:
                        full(dve, ("in_z", 1, KI - 1))
                    if j == 0 and c + mlp > 0:
                        full(dve, ("down", c if mlp else c - 1, 1 - mlp, KD - 1))
                    nc.vector.scalar_tensor_tensor(out=gated[:, j, :], in0=gs[:, :], scalar=0.5, in1=bank((s, "up")),
                                                   op0=ALU.mult, op1=ALU.mult).then_inc(gated_done, 1)
                    dve.wait_ge(gated_done, HT * (2 * c + mlp) + j + 1)
                    dve.sem_inc(free_of((s, "up")), 1)
                elif kind == "down":
                    mlp, o = s[2], s[3]
                    full(dve, s)
                    if mlp == 0:
                        link(nc.vector.tensor_tensor(a[:, c, o, :], a[:, c, o, :], bank(s), ALU.add))
                        dve.sem_inc(free_of(s), 1)
                        nc.vector.tensor_tensor(h[:, c, o, :], h[:, c, o, :], a[:, c, o, :], ALU.add).then_inc(h1_done, 1)
                    else:
                        nc.vector.tensor_tensor(h[:, c, o, :], h[:, c, o, :], bank(s), ALU.add).then_inc(final_done, 1)
                        dve.wait_ge(final_done, KD * c + o + 1)
                        dve.sem_inc(free_of(s), 1)

            for unit, steps in slots:
                if unit is not None:
                    scan(unit)
                for s in steps:
                    step(s)

        @block.tensor
        def _(pe):
            def product(name, pairs):
                n = uses[name]
                if n >= NG:
                    pe.wait_ge(bank_free[n % NG], n // NG)
                for k, (w, x) in enumerate(pairs):
                    last = nc.tensor.matmul(work[n % NG][:, 0:T], w, x, start=(k == 0), stop=(k == len(pairs) - 1))
                last.then_inc(bank_full[n % NG], 1)

            def c_broadcast(u):
                c, m, q = u // UNITS, u % UNITS // QU, u % QU
                pe.wait_ge(c_ready, KI * c + m + 1)
                for half in range(2):
                    if u >= 1:
                        pe.wait_ge(c_free, 2 * (u - 1) + half + 1)
                    for i in range(2):
                        lo = S_PICKC + (2 * half + i) * P
                        rows = slice(32 * q, 32 * q + 32)
                        last = nc.tensor.matmul(cps[half][:, i, 0:T], sm[rows, lo:lo + P], cm[rows, m, :],
                                                start=True, stop=True)
                    last.then_inc(c_full, 1)

            def weights(c, mlp, i):
                n = load_index(c, mlp, i)
                pe.wait_ge(w_loaded[n % NW], 16 * (n // NW + 1))
                return wring[:, n % NW, :]

            def step(s):
                kind, c = s[0], s[1]
                if kind == "tok":
                    if c == 0:
                        pe.wait_ge(pat_loaded, 16)
                        pe.wait_ge(tokw_loaded, 16)
                    for k in range(KD):
                        product(("tok", c, k), [(tokw[:, k * P:(k + 1) * P], pat[:, c, :])])
                elif kind in ("ln1_mean", "ln2_mean"):
                    if kind == "ln1_mean":
                        pe.wait_ge(consts_done, 1)
                        pe.wait_ge(h_done, KD * (c + 1))
                    else:
                        pe.wait_ge(h1_done, KD * (c + 1))
                    product(s, [(mean_w[:, :], h[:, c, k, :]) for k in range(KD)])
                elif kind in ("ln1_var", "ln2_var", "rms1", "rms2"):
                    pe.wait_ge(sq_done, norm_index(kind[0:3] if kind[0] == "l" else kind, c) + 1)
                    product(s, [(mean_w[:, :], sq[:, k, :]) for k in range(KD)])
                elif kind in ("in_dt", "in_x", "in_b", "in_c", "in_z"):
                    t = {"in_dt": IN_DT, "in_x": IN_X + s[-1], "in_b": IN_B + s[-1], "in_c": IN_CZ + 2 * s[-1],
                         "in_z": IN_CZ + 2 * s[-1] + 1}[kind]
                    if kind == "in_dt":
                        pe.wait_ge(norm_done, norm_index("rms1", c) + 1)
                    if c == 0:
                        for g, (lo, hi) in enumerate(IN_GROUPS):
                            if lo == t:
                                pe.wait_ge(win_loaded[g], 16)
                    product(s, [(win[:, t, k * P:(k + 1) * P], hn[:, k, :]) for k in range(KD)])
                elif kind == "dtp":
                    if c == 0 and s[2] == 0:
                        pe.wait_ge(wdt_loaded, 16)
                    pe.wait_ge(dti_done, c + 1)
                    product(s, [(wdt[:, s[2] * P:(s[2] + 1) * P], dti[:, :])])
                elif kind == "xs":
                    m = s[2]
                    if c == 0 and m == 0:
                        pe.wait_ge(small_loaded, 16)
                    pe.wait_ge(xv_done, 2 * c + m // 4 + 1)
                    rows = slice(32 * (m % 4), 32 * (m % 4) + 32)
                    product(s, [(sm[rows, S_PICKX:S_PICKX + P], xv[rows, m // 4, :])])
                elif kind == "out":
                    if c == 0 and s[2] == 0:
                        pe.wait_ge(wout_loaded, 16)
                    pe.wait_ge(y_done, KI * (c + 1))
                    product(s, [(wout[:, m, s[2] * P:(s[2] + 1) * P], yg[:, m, :]) for m in range(KI)])
                elif kind == "gu":
                    mlp, j = s[2], s[3]
                    if j == 0:
                        pe.wait_ge(norm_done, norm_index(("rms2", "ln2")[mlp], c) + 1)
                    w = weights(c, mlp, j)
                    product((s, "gate"), [(w[:, k * P:(k + 1) * P], hn[:, k, :]) for k in range(KD)])
                    product((s, "up"), [(w[:, (KD + k) * P:(KD + k + 1) * P], hn[:, k, :]) for k in range(KD)])
                elif kind == "down":
                    mlp, o = s[2], s[3]
                    pe.wait_ge(gated_done, HT * (2 * c + mlp + 1))
                    ws = [weights(c, mlp, HT + 2 * o + half) for half in range(2)]
                    product(s, [(ws[j // 8][:, (j % 8) * P:(j % 8 + 1) * P], gated[:, j, :]) for j in range(HT)])

            for unit, steps in slots:
                if unit is not None:
                    c_broadcast(unit)
                for s in steps:
                    step(s)


def kernel(**inputs):
    import numpy as np
    import concourse.bacc as bacc
    from concourse.bass_utils import run_bass_kernel_spmd

    g = {k: np.asarray(v) for k, v in inputs.items()}
    f = np.float32

    def cols(v, n):
        return v.reshape(n, P).T

    x = g["x"][:, :, 0]
    starts = [i * HOP for i in range(STEPS)]
    assert starts[-1] + PATCH <= SERIES < starts[-1] + HOP + PATCH
    pat = np.stack([x[:, s:s + PATCH] for s in starts], 1).reshape(BATCH * STEPS, PATCH).T
    pat = pat.reshape(P, NCH, T)

    wi = g["L0_attn_in_proj_w"]
    z0, x0, b0, c0, d0 = 0, DI, DI + XB, DI + 2 * XB, 2 * DI + 2 * XB
    starts = [d0, x0, x0 + P, b0, b0 + P]
    for m in range(KI):
        starts += [c0 + m * P, z0 + m * P]
    by_state = np.arange(P).reshape(P // NS, NS).T.ravel()
    order = {s: (s + by_state if c0 <= s < c0 + DI else s + np.arange(P)) for s in starts}
    w_in = np.stack([wi[order[s]].T.reshape(KD, P, P).transpose(1, 0, 2).reshape(P, D) for s in starts], 1)

    row, ch = np.arange(P)[:, None] % 32, np.arange(P)[None, :]
    pick_x = (row == 16 * (ch // 64) + ch % 16).astype(f)
    pick_c = np.concatenate([row == (P // NS) * i + ch // 16 for i in range(NQ)], 1).astype(f)
    small = np.concatenate([
        cols(g["L0_tok_b"], KD), cols(g["L0_attn_dt_proj_b"], KI), cols(g["L0_attn_D_skip"], KI),
        cols(g["L0_attn_rms1_w"], KD), cols(g["L0_attn_rms2_w"], KD),
        g["L0_attn_A_log"].reshape(KI, P, NS).transpose(1, 0, 2).reshape(P, KI * NS), pick_x, pick_c], 1)

    def mlp(gate, up, down):
        gt = gate.T.reshape(KD, P, HT, P).transpose(2, 1, 0, 3).reshape(HT, P, D)
        ut = up.T.reshape(KD, P, HT, P).transpose(2, 1, 0, 3).reshape(HT, P, D)
        gu = np.concatenate([gt, ut], 2)
        dn = down.reshape(KD, P, 2, HT // 2, P).transpose(0, 2, 4, 3, 1).reshape(2 * KD, P, WSLOT)
        return [gu, dn]

    w_mlp = np.concatenate(mlp(g["L0_attn_gate_w"], g["L0_attn_up_w"], g["L0_attn_down_w"])
                           + mlp(g["L0_ffn_w_gate"], g["L0_ffn_w_up"], g["L0_ffn_w_down"]), 0)
    arrays = {
        "patches": pat, "tok_w": g["L0_tok_W"].T, "small": small, "w_in": w_in, "w_dt": g["L0_attn_dt_proj_w"].T,
        "w_out": g["L0_attn_out_proj_w"].T.reshape(KI, P, D).transpose(1, 0, 2), "w_mlp": w_mlp}
    arrays = {k: np.ascontiguousarray(v) for k, v in arrays.items()}

    nc = bacc.Bacc("TRN2", target_bir_lowering=False, num_devices=1)
    aps = [nc.dram_tensor(k, v.shape, mybir.dt.from_np(v.dtype), kind="ExternalInput").ap() for k, v in arrays.items()]
    out = nc.dram_tensor("out", (D, BATCH * STEPS), F32, kind="ExternalOutput").ap()
    build(nc, *aps, out)
    r = run_bass_kernel_spmd(nc, [arrays], core_ids=[0])
    return np.ascontiguousarray(r.results[0]["out"].T).reshape(BATCH, STEPS, D)
```

```python
from contextlib import ExitStack

import concourse.bass as bass
from concourse import mybir

F32 = mybir.dt.float32
F32R = mybir.dt.float32r
ALU = mybir.AluOpType
ACT = mybir.ActivationFunctionType

P = 128
BATCH, SERIES = 64, 750
PATCH, HOP = 128, 64
STEPS = (SERIES - PATCH) // HOP + 1
D = 512
DI = 1024
XB = 256
NS = 16
HID = 2048
EPS = 1e-5

NCH = 2
CB = BATCH // NCH
T = CB * STEPS
KD = D // P
KI = DI // P
HT = HID // P
NQ = 4
QU = NS // NQ
UNITS = KI * QU
BANK = 512

IN_DT, IN_X, IN_B, IN_CZ = 0, 1, 3, 5
IN_TILES = 5 + 2 * KI
IN_GROUPS = [(0, 5), (5, 9), (9, 13), (13, 17), (17, 21)]

S_TOKB, S_DTB, S_DSKIP, S_W1, S_W2 = 0, 4, 12, 20, 24
S_ALOG = 28
S_PICKX = S_ALOG + KI * NS
S_IDENT = S_PICKX + P
S_COLS = S_IDENT + P

NH, NB, ND, NC, NG = 4, 3, 2, 2, 4
HALVED = (1, 3)
WSLOT = 2 * D
KEEP_CLOCK = 14
DVE_SHARE = 6
MIXED_FROM = UNITS + 5
NRAW, NW = 4, 3
HH = HT // 2
SPLITS = 4 * (HH + KD)
LOADS = KD + SPLITS


def a_steps(c):
    norm = [("tok", c), ("ln1_mean", c), ("ln1_var", c), ("rms1", c)]
    tiles = [[("dtp", c, m), ("xs", c, m), ("in_c", c, m), ("in_z", c, m)] for m in range(KI)]
    first = [("in_dt", c), ("in_b", c, 0), ("in_x", c, 0), ("in_b", c, 1), ("in_x", c, 1)]
    return norm, first, tiles


def m_steps(c):
    s = [("out", c, o) for o in range(KD)] + [("rms2", c)]
    for mlp in range(2):
        if mlp == 1:
            s += [("ln2_mean", c), ("ln2_var", c)]
        for half in range(2):
            s += [("gu", c, mlp, half, j) for j in range(HH)] + [("down", c, mlp, half, o) for o in range(KD)]
    return s


def schedule():
    norm0, first0, tiles0 = a_steps(0)
    norm1, first1, tiles1 = a_steps(1)
    dtp, xs, in_c, in_z = tiles0[0]
    slots = [(None, norm0 + first0[0:3] + [dtp, xs, in_c, in_z]), (None, first0[3:])]
    bg = [half for t in tiles0[1:] for half in (t[0::2], t[1::2])]
    bg += [norm1[0:2], norm1[2:3], norm1[3:4], first1]
    bg += [half for t in tiles1[:KI - 1] for half in (t[0::2], t[1::2])]
    assert len(bg) == UNITS
    slots += list(enumerate(bg))
    steps = m_steps(0)
    dtp, xs, in_c, in_z = tiles1[KI - 1]
    first = [[in_c, in_z], steps[0:1], steps[1:2] + [dtp], steps[2:3], steps[3:4] + [xs], steps[4:5]]
    rest, left = steps[5:], UNITS - len(first)
    for u, bg in enumerate(first):
        slots.append((UNITS + u, bg))
    for u in range(left):
        slots.append((UNITS + len(first) + u, rest[len(rest) * u // left:len(rest) * (u + 1) // left]))
    slots.append((None, m_steps(1)))
    return slots


LATE = ("dtp", "xs", "in_c", "in_z", "out")


def late(slots, lag):
    def lag_of(i, s):
        return lag if i == 1 or (s[0] in LATE and slots[i][0] is not None) else 0
    return [(unit, [s for j in range(max(0, i - lag), i + 1) for s in slots[j][1] if lag_of(j, s) == i - j])
            for i, (unit, _) in enumerate(slots)]


def work_bank_uses():
    uses, counts, turn, banks = {}, [0] * NG, 0, NG - 1
    for unit, steps in schedule():
        if unit == UNITS:
            banks, turn = NG, NG - 1
        for s in steps:
            names = {"tok": [("tok", s[1], k) for k in range(KD)],
                     "gu": [(s, "gate"), (s, "up")]}.get(s[0], [s])
            for n in names:
                b = turn % banks
                uses[n] = (b, counts[b])
                counts[b] += 1
                turn += 1
    return uses


def build(nc, patches, tok_w, small, pick, w_in, w_dt, w_stream, out):
    slots = schedule()
    uses = work_bank_uses()
    silus = {s: i for i, s in enumerate(s for _, steps in slots for s in steps if s[0] in ("in_z", "gu"))}
    readers = [s for _, steps in slots for s in steps if s[0] in ("out", "gu", "down")]
    load_of = {s: i for i, s in enumerate(readers)}
    split_loads = [i for i, s in enumerate(readers) if s[0] != "out"]
    split_of = {readers[i]: k for k, i in enumerate(split_loads)}
    c_dram = nc.dram_tensor("c_rows", (NCH * KI, 2, P, T), F32, kind="Internal").ap()
    b_dram = nc.dram_tensor("b_rows", (NCH, XB, T), F32, kind="Internal").ap()

    with ExitStack() as ctx:
        def sb(name, shape, dtype=F32):
            return ctx.enter_context(nc.sbuf_tensor(name, shape, dtype))

        def sem(name):
            return ctx.enter_context(nc.semaphore(name))

        sm = sb("sm", [P, S_COLS])
        a_neg = sb("a_neg", [P, KI * NS])
        mean_w = sb("mean_w", [P, P])
        pick_c = sb("pick_c", [P, NQ * P], F32R)
        h = sb("h", [P, NCH, KD, T])
        a = sb("a", [P, NCH, KD, T])
        sq = sb("sq", [P, KD, T])
        xv = sq[:, 0:2, :]
        bs = sq[:, 2:4, :]
        rstd_ln = sb("rstd_ln", [P, T])
        rstd = sb("rstd", [P, T])
        dt = sb("dt", [P, KI, T])
        xf = sb("xf", [P, KI, T])
        z = sb("z", [P, KI, T])
        yg = sb("yg", [P, KI, T])
        c_part = sb("c_part", [P, 2, T], F32R)
        c_st = sb("c_st", [P, NC, 2, T], F32R)
        pair = sb("pair", [P, 2, T])
        sp_u, sp_l = pair[:, 0, :], pair[:, 1, :]
        gated_f = pair
        sp_e = sb("sp_e", [P, T])
        gate2 = sp_e
        th = sb("th", [P, 2, T])
        dtx = sb("dtx", [P, 2, T])
        bb = sb("bb", [P, NB, NQ * T])
        da = sb("da", [P, ND, NQ * T])
        hs = sb("hs", [P, NH, NQ, T])
        acc = sb("acc", [P, 2, T])
        ysum = sb("ysum", [P, T])
        eps_col = sb("eps_col", [P, 1])
        eps_ap = eps_col[:, :]

        with ExitStack() as prep:
            def sb_prep(name, shape):
                return prep.enter_context(nc.sbuf_tensor(name, shape, F32))

            pat = sb_prep("pat", [P, NCH, T])
            tokw = sb_prep("tokw", [P, D])
            win = sb_prep("win", [P, IN_TILES, D])
            wdt = sb_prep("wdt", [P, DI])
            hn = sb_prep("hn", [P, KD, T])
            dti = sb_prep("dti", [P, T])
            pick_in = sb_prep("pick_in", [P, NQ * P])
        wraw = sb("wraw", [P, NRAW, WSLOT])
        ws = sb("ws", [P, NW, 2, WSLOT], F32R)
        hn2 = sb("hn2", [P, 2, KD, T], F32R)
        gated = sb("gated", [P, 2, HH, T], F32R)

        work = [ctx.enter_context(nc.psum_tensor(f"work{i}", [P, BANK], F32)) for i in range(NG)]
        cps = [ctx.enter_context(nc.psum_tensor(f"c_bcast{i}", [P, 2, BANK], F32)) for i in range(2)]

        pat_loaded, tokw_loaded, small_loaded = sem("pat_loaded"), sem("tokw_loaded"), sem("small_loaded")
        win_loaded = [sem(f"win_loaded{g}") for g in range(len(IN_GROUPS))]
        wdt_loaded = sem("wdt_loaded")
        w_loaded = [sem(f"w_loaded{i}") for i in range(NRAW)]
        w_hi_done, w_lo_pool, w_lo_dve = sem("w_hi_done"), sem("w_lo_pool"), sem("w_lo_dve")
        c_hi_done, c_lo_done, c_stored = sem("c_hi_done"), sem("c_lo_done"), sem("c_stored")
        c_loaded = [sem(f"c_loaded{i}") for i in range(NC)]
        pick_loaded, pick_done = sem("pick_loaded"), sem("pick_done")
        hn2_hi, hn2_lo = sem("hn2_hi"), sem("hn2_lo")
        gated_raw, gated_hi, gated_lo = sem("gated_raw"), sem("gated_hi"), sem("gated_lo")
        bb_loaded = [sem(f"bb_loaded{i}") for i in range(NB)]
        b_stored = sem("b_stored")
        out_stored = sem("out_stored")
        consts_done = sem("consts_done")
        a_neg_exp = sem("a_neg_exp")
        a_neg_done = sem("a_neg_done")
        bank_full = [sem(f"bank_full{i}") for i in range(NG)]
        bank_free = [sem(f"bank_free{i}") for i in range(NG)]
        h_done = sem("h_done")
        centered = sem("centered")
        sq_done = sem("sq_done")
        rstd_done = sem("rstd_done")
        norm_done = sem("norm_done")
        dti_done, xv_done, bs_done = sem("dti_done"), sem("xv_done"), sem("bs_done")
        sp_act = sem("sp_act")
        halved_done, h_summed, sum_done, sum_read = sem("halved_done"), sem("h_summed"), sem("sum_done"), sem("sum_read")
        sp_rest, sp_small = sem("sp_rest"), sem("sp_small")
        dt_ready, x_ready, z_ready = sem("dt_ready"), sem("x_ready"), sem("z_ready")
        th_done, th_used = sem("th_done"), sem("th_used")
        dtx_done, dbx_done, da_done, da_zeroed = sem("dtx_done"), sem("dbx_done"), sem("da_done"), sem("da_zeroed")
        scan_done, h_used, y_done = sem("scan_done"), sem("h_used"), sem("y_done")
        c_full, c_free = sem("c_full"), sem("c_free")
        res_done = sem("res_done")
        h1_done, final_done = sem("h1_done"), sem("final_done")
        dve_chain = sem("dve_chain")

        def bank(name):
            return work[uses[name][0]][:, 0:T]

        def full(eng, name):
            name = (name, "up") if name[0] == "gu" else name
            b, n = uses[name]
            eng.wait_ge(bank_full[b], n + 1)

        def free_of(name):
            return bank_free[uses[name][0]]

        def small_ap(col, i):
            return sm[:, col + i:col + i + 1]

        def norm_index(name, c):
            return [("ln1", 0), ("rms1", 0), ("ln1", 1), ("rms1", 1), ("rms2", 0), ("ln2", 0), ("rms2", 1),
                    ("ln2", 1)].index((name, c))

        def ln_index(name, c):
            return [("ln1", 0), ("ln1", 1), ("ln2", 0), ("ln2", 1)].index((name, c))

        def tile_of(s):
            return HH * (4 * s[1] + 2 * s[2] + s[3]) + s[4]

        def down_step(half, o):
            return ("down", half // 4, half // 2 % 2, half % 2, o)

        def mlp_norm(c, mlp):
            return 2 * c + mlp

        def on_dve(k):
            return k % DVE_SHARE == DVE_SHARE - 1

        def low_part(eng, k):
            n = len([i for i in range(k + 1) if on_dve(i) == on_dve(k)])
            eng.wait_ge(w_lo_dve if on_dve(k) else w_lo_pool, n)

        def splits_at(s):
            if s[0] == "out":
                return range(SPLITS * s[1], SPLITS * s[1] + NW - 1) if s[2] == KD - 2 else []
            if s in split_of and split_of[s] % SPLITS < SPLITS - NW + 1:
                return [split_of[s] + NW - 1]
            return []

        block = ctx.enter_context(nc.Block())

        @block.sync
        def _(sp):
            sp.dma_start(pat[:, :, :], patches).then_inc(pat_loaded, 16)
            sp.dma_start(tokw[:, :], tok_w).then_inc(tokw_loaded, 16)
            sp.dma_start(sm[:, :], small).then_inc(small_loaded, 16)
            sp.dma_start(pick_in[:, :], pick).then_inc(pick_loaded, 16)
            for g, (lo, hi) in enumerate(IN_GROUPS):
                sp.dma_start(win[:, lo:hi, :], w_in[:, lo:hi, :]).then_inc(win_loaded[g], 16)
                if g == 0:
                    sp.dma_start(wdt[:, :], w_dt).then_inc(wdt_loaded, 16)

            def load_b(u):
                c, m, q = u // UNITS, u % UNITS // QU, u % QU
                if u >= NB:
                    sp.wait_ge(dbx_done, u - NB + 1)
                if u % UNITS in (0, UNITS // 2):
                    sp.wait_ge(b_stored, 16 * (2 * c + 2 * m // KI + 1))
                rows = b_dram[c].rearrange("(g n) t -> g (n t)", n=NS)
                for g in range(2):
                    src = rows[2 * m + g:2 * m + g + 1, q * NQ * T:(q + 1) * NQ * T].to_broadcast([64, NQ * T])
                    sp.dma_start(bb[64 * g:64 * g + 64, u % NB, :], src).then_inc(bb_loaded[u % NB], 16)

            def load_c(t):
                sp.wait_ge(c_stored, 16 * (t + 1))
                if t >= NC:
                    sp.wait_ge(c_full, 2 * QU * (t - NC + 1))
                for odd in range(2):
                    for part in range(2):
                        src = c_dram[t, part].rearrange("(k o r) t -> o r k t", o=2, r=32)[odd]
                        lo = 64 * odd + 32 * part
                        sp.dma_start(c_st[lo:lo + 32, t % NC, :, :].bitcast(F32), src).then_inc(c_loaded[t % NC], 16)

            def load_w(i):
                if i >= len(readers):
                    return
                if i == 0:
                    full(sp, ("in_z", 1, 0))
                if i >= NRAW:
                    if readers[i - NRAW][0] == "out":
                        full(sp, readers[i - NRAW])
                    else:
                        low_part(sp, split_of[readers[i - NRAW]])
                sp.dma_start(wraw[:, i % NRAW, :], w_stream[i % LOADS]).then_inc(w_loaded[i % NRAW], 16)

            for unit, steps in late(slots, 1):
                if unit is not None and unit + NB - 1 < NCH * UNITS:
                    load_b(unit + NB - 1)
                for s in steps:
                    if s[0] == "in_b":
                        c, i = s[1:]
                        sp.wait_ge(bs_done, 2 * c + i + 1)
                        sp.dma_start(b_dram[c, i * P:(i + 1) * P, :], bs[:, i, :]).then_inc(b_stored, 16)
                        if c + i == 0:
                            for u in range(NB - 1):
                                load_b(u)
                    if s == ("in_c", 0, 0):
                        load_c(0)
                    if s == ("in_z", 1, 0):
                        for i in range(NRAW):
                            load_w(i)
                    if s in load_of and load_of[s] >= 1:
                        load_w(load_of[s] + NRAW - 1)
                if unit is not None and unit % QU == QU // 2 and unit // QU + 1 < NCH * KI:
                    load_c(unit // QU + 1)
            for c in range(NCH):
                for o in range(KD):
                    sp.wait_ge(final_done, KD * c + o + 1)
                    sp.dma_start(out[o * P:(o + 1) * P, c * T:(c + 1) * T], h[:, c, o, :]).then_inc(out_stored, 16)
            sp.wait_ge(out_stored, 16 * NCH * KD)

        @block.gpsimd
        def _(pool):
            nc.gpsimd.memset(da[:, :, :], 0.0).then_inc(da_zeroed, 1)
            def split_low(k):
                pool.wait_ge(w_hi_done, k + 1)
                nc.gpsimd.tensor_tensor(ws[:, k % NW, 1, :], wraw[:, split_loads[k] % NRAW, :],
                                        ws[:, k % NW, 0, :].bitcast(F32), ALU.subtract).then_inc(w_lo_pool, 1)

            def input_term(u):
                c, m, q = u // UNITS, u % UNITS // QU, u % QU
                t = c * KI + m
                if q == 0:
                    pool.wait_ge(dt_ready, t + 1)
                    pool.wait_ge(x_ready, t + 1)
                    if t >= 2:
                        pool.wait_ge(dbx_done, QU * (t - 1))
                    nc.gpsimd.tensor_tensor(dtx[:, t % 2, :], dt[:, m, :], xf[:, m, :], ALU.mult).then_inc(dtx_done, 1)
                    pool.wait_ge(dtx_done, t + 1)
                pool.wait_ge(bb_loaded[u % NB], 32 * (u // NB + 1))
                if u >= NH:
                    if u - NH < UNITS:
                        pool.wait_ge(h_summed, u - NH + 1)
                    else:
                        pool.wait_ge(h_used, u - NH - UNITS + 1)
                nc.gpsimd.tensor_tensor(hs[:, u % NH, :, :], dtx[:, t % 2, :].unsqueeze(1).to_broadcast([P, NQ, T]),
                                        bb[:, u % NB, :].rearrange("p (n t) -> p n t", t=T),
                                        ALU.mult).then_inc(dbx_done, 1)

            def softplus(c, m):
                i = KI * c + m
                pool.wait_ge(sp_rest, i + 1)
                nc.gpsimd.tensor_tensor(sp_u[:, :], sp_u[:, :], sp_l[:, :], ALU.add).then_inc(sp_small, 1)
                pool.wait_ge(sp_small, i + 1)
                nc.gpsimd.tensor_tensor(dt[:, m, :], dt[:, m, :], sp_u[:, :], ALU.add).then_inc(dt_ready, 1)

            for unit, steps in late(slots, 2):
                if unit is not None:
                    input_term(unit)
                for s in steps:
                    if s[0] == "dtp":
                        softplus(s[1], s[2])
                    for k in splits_at(s):
                        if not on_dve(k):
                            split_low(k)

        @block.scalar
        def _(act):
            tables = [""]

            def log_tables():
                if tables[0] != "log":
                    nc.scalar.preload_act_table_set("natural_log_exp_and_others")
                    tables[0] = "log"

            log_tables()
            act.wait_ge(small_loaded, 16)
            nc.scalar.activation(a_neg[:, :], sm[:, S_ALOG:S_ALOG + KI * NS], ACT.Exp).then_inc(a_neg_exp, 1)

            def decay(u):
                c, m, q = u // UNITS, u % UNITS // QU, u % QU
                if u == 0:
                    act.wait_ge(da_zeroed, 1)
                    act.wait_ge(a_neg_done, 1)
                act.wait_ge(dt_ready, c * KI + m + 1)
                if u >= ND:
                    act.wait_ge(scan_done, u - ND + 1)
                src = dt[:, m, :].rearrange("p (b t) -> p b t", t=STEPS)[:, :, 1:]
                for i in range(NQ):
                    dst = da[:, u % ND, i * T:(i + 1) * T].rearrange("p (b t) -> p b t", t=STEPS)[:, :, 1:]
                    n = m * NS + q * NQ + i
                    last = nc.scalar.activation(dst, src, ACT.Exp, scale=a_neg[:, n:n + 1])
                last.then_inc(da_done, 1)

            def split_high(k):
                i = split_loads[k]
                act.wait_ge(w_loaded[i % NRAW], 16 * (i // NRAW + 1))
                if k >= NW:
                    full(act, readers[split_loads[k - NW]])
                nc.scalar.copy(ws[:, k % NW, 0, :], wraw[:, i % NRAW, :]).then_inc(w_hi_done, 1)

            def hn2_high(c, mlp):
                n, v = mlp_norm(c, mlp), norm_index(("rms2", "ln2")[mlp], c)
                if n >= 1:
                    full(act, ("gu", (n - 1) // 2, (n - 1) % 2, 1, HH - 1))
                for k in range(KD):
                    act.wait_ge(norm_done, KD * v + k + 1)
                    nc.scalar.copy(hn2[:, 0, k, :], sq[:, k, :]).then_inc(hn2_hi, 1)

            def gated_high(n):
                act.wait_ge(gated_raw, n + 1)
                if n % HH == 0 and n >= HH:
                    full(act, down_step(n // HH - 1, KD - 1))
                nc.scalar.copy(gated[:, 0, n % HH, :], gated_f[:, n % 2, :]).then_inc(gated_hi, 1)

            def squares(x, v, written, count):
                log_tables()
                stored = {2: 2, 4: 4}.get(v, 0)
                if stored:
                    act.wait_ge(b_stored, 16 * stored)
                for k in range(KD):
                    act.wait_ge(written, KD * count + k + 1)
                    nc.scalar.activation(sq[:, k, :], x[:, k, :], ACT.Square).then_inc(sq_done, 1)

            def inverse_root(name, v):
                full(act, name)
                nc.scalar.activation(rstd_ln[:, :], bank(name), ACT.Ln, bias=eps_ap).then_inc(free_of(name), 1)
                act.wait_ge(free_of(name), uses[name][1] + 1)
                if v >= 1:
                    act.wait_ge(norm_done, KD * v)
                nc.scalar.activation(rstd[:, :], rstd_ln[:, :], ACT.Exp, scale=-0.5).then_inc(rstd_done, 1)

            def step(s):
                kind, c = s[0], s[1]
                if kind == "tok":
                    for k in range(KD):
                        full(act, ("tok", c, k))
                        nc.scalar.activation(h[:, c, k, :], bank(("tok", c, k)), ACT.Identity,
                                             bias=small_ap(S_TOKB, k)).then_inc(free_of(("tok", c, k)), 1)
                        act.wait_ge(free_of(("tok", c, k)), uses[("tok", c, k)][1] + 1)
                        act.sem_inc(h_done, 1)
                elif kind == "ln1_var":
                    squares(a[:, c, :, :], norm_index("ln1", c), centered, ln_index("ln1", c))
                    inverse_root(s, norm_index("ln1", c))
                elif kind == "rms1":
                    squares(a[:, c, :, :], norm_index("rms1", c), norm_done, norm_index("ln1", c))
                    inverse_root(s, norm_index("rms1", c))
                elif kind == "rms2":
                    squares(a[:, c, :, :], norm_index("rms2", c), res_done, c)
                    inverse_root(s, norm_index("rms2", c))
                    hn2_high(c, 0)
                elif kind == "ln2_var":
                    squares(a[:, c, :, :], norm_index("ln2", c), centered, ln_index("ln2", c))
                    inverse_root(s, norm_index("ln2", c))
                    hn2_high(c, 1)
                elif kind == "in_c":
                    t = KI * c + s[2]
                    if t >= 1:
                        act.wait_ge(c_stored, 16 * t)
                    full(act, s)
                    nc.scalar.copy(c_part[:, 0, :], bank(s)).then_inc(c_hi_done, 1)
                elif kind in ("in_dt", "in_x", "in_b", "xs"):
                    dst, done = {"in_dt": lambda: (dti[:, :], dti_done), "in_x": lambda: (xv[:, s[2], :], xv_done),
                                 "in_b": lambda: (bs[:, s[2], :], bs_done), "xs": lambda: (xf[:, s[2], :], x_ready)}[kind]()
                    if kind == "xs" and c >= 1:
                        act.wait_ge(y_done, KI * (c - 1) + s[2] + 1)
                    full(act, s)
                    nc.scalar.copy(dst, bank(s)).then_inc(done, 1)
                    act.wait_ge(done, {"in_dt": c + 1, "in_x": 2 * c + s[-1] + 1, "in_b": 2 * c + s[-1] + 1}.get(
                        kind, KI * c + s[-1] + 1))
                    act.sem_inc(free_of(s), 1)
                elif kind == "in_z":
                    silu(s, s)
                elif kind == "dtp":
                    m = s[2]
                    i = KI * c + m
                    if c >= 1:
                        act.wait_ge(y_done, KI * (c - 1) + m + 1)
                    log_tables()
                    if i >= 1:
                        act.wait_ge(dt_ready, i)
                    full(act, s)
                    nc.scalar.activation(dt[:, m, :], bank(s), ACT.Relu, bias=small_ap(S_DTB, m))
                    nc.scalar.activation(sp_u[:, :], bank(s), ACT.Abs, bias=small_ap(S_DTB, m)).then_inc(free_of(s), 1)
                    act.wait_ge(free_of(s), uses[s][1] + 1)
                    nc.scalar.activation(sp_u[:, :], sp_u[:, :], ACT.Exp, scale=-1.0).then_inc(sp_act, 1)
                    act.wait_ge(sp_act, 2 * i + 1)
                    nc.scalar.activation(sp_l[:, :], sp_u[:, :], ACT.Ln, bias=1.0).then_inc(sp_act, 1)
                elif kind == "gu":
                    silu(s, (s, "gate"))
                    n, j = tile_of(s), s[4]
                    if j >= 1:
                        gated_high(n - 1)
                    if j == HH - 1:
                        gated_high(n)

            def silu(s, name):
                i = silus[s]
                full(act, name)
                if i >= 2:
                    act.wait_ge(th_used, i - 1)
                tables[0] = "tanh"
                nc.scalar.activation(th[:, i % 2, :], bank(name), ACT.Tanh, scale=0.5).then_inc(th_done, 1)

            def store_c(t):
                act.wait_ge(c_lo_done, t + 1)
                act.dma_start(c_dram[t].rearrange("i p t -> p i t"), c_part[:, :, :].bitcast(F32)).then_inc(c_stored, 16)

            act_slots = late(slots, 1)
            for i, (unit, steps) in enumerate(act_slots):
                if unit == 0:
                    decay(0)
                if unit is not None and unit + 1 < NCH * UNITS:
                    decay(unit + 1)
                for s in act_slots[i - 1][1] if i else []:
                    if s[0] == "in_c":
                        store_c(KI * s[1] + s[2])
                for s in steps:
                    for k in splits_at(s):
                        split_high(k)
                    step(s)

        @block.vector
        def _(dve):
            chain = [0]

            def link(ins):
                chain[0] += 1
                ins.then_inc(dve_chain, 1)
                dve.wait_ge(dve_chain, chain[0])

            nc.vector.memset(eps_ap, EPS)
            nc.vector.memset(mean_w[:, :], 1.0 / D).then_inc(consts_done, 1)
            dve.wait_ge(pick_loaded, 16)
            nc.vector.tensor_copy(pick_c[:, :], pick_in[:, :]).then_inc(pick_done, 1)
            dve.wait_ge(a_neg_exp, 1)
            nc.vector.tensor_scalar(a_neg[:, :], a_neg[:, :], -1.0, None, ALU.mult).then_inc(a_neg_done, 1)

            def scan(u):
                flat = hs[:, u % NH, :, :].rearrange("p n t -> p (n t)")
                dve.wait_ge(dbx_done, u + 1)
                dve.wait_ge(da_done, u + 1)
                nc.vector.tensor_tensor_scan(flat, da[:, u % ND, :], flat, 0.0, ALU.mult, ALU.add).then_inc(scan_done, 1)

            def times_c(u):
                dve.wait_ge(scan_done, u + 1)
                for half in range(2):
                    pair = hs[:, u % NH, 2 * half:2 * half + 2, :]
                    dve.wait_ge(c_full, 2 * u + half + 1)
                    nc.vector.tensor_tensor(pair, pair, cps[half][:, :, 0:T], ALU.mult).then_inc(c_free, 1)

            def add_states(u):
                c, m, q = u // UNITS, u % UNITS // QU, u % QU
                slot = hs[:, u % NH, :, :]
                dve.wait_ge(c_free, 2 * u + 2)
                if c == 0:
                    if q in HALVED:
                        nc.vector.tensor_tensor(slot[:, 0:2, :], slot[:, 0:2, :], slot[:, 2:4, :],
                                                ALU.add).then_inc(halved_done, 1)
                elif q == 0:
                    nc.vector.tensor_tensor(acc[:, :, :], slot[:, 0:2, :], slot[:, 2:4, :], ALU.add).then_inc(h_used, 1)
                else:
                    link(nc.vector.tensor_tensor(acc[:, :, :], acc[:, :, :], slot[:, 0:2, :], ALU.add))
                    nc.vector.tensor_tensor(acc[:, :, :], acc[:, :, :], slot[:, 2:4, :], ALU.add).then_inc(h_used, 1)
                if c == 1:
                    dve.wait_ge(h_used, u - UNITS + 1)
                    if q == QU - 1:
                        link(nc.vector.tensor_tensor(ysum[:, :], acc[:, 0, :], acc[:, 1, :], ALU.add))

            def gate_y(t):
                c, m = t // KI, t % KI
                total = work[NG - 1][:, 0:T] if c == 0 else ysum[:, :]
                dve.wait_ge(x_ready, t + 1)
                if c == 0:
                    dve.wait_ge(sum_done, t + 1)
                nc.vector.scalar_tensor_tensor(out=ysum[:, :], in0=xf[:, m, :], scalar=small_ap(S_DSKIP, m),
                                               in1=total, op0=ALU.mult, op1=ALU.add).then_inc(sum_read, 1)
                dve.wait_ge(sum_read, t + 1)
                dve.wait_ge(z_ready, t + 1)
                if c >= 1:
                    full(dve, ("out", c - 1, KD - 1))
                nc.vector.scalar_tensor_tensor(out=yg[:, m, :], in0=ysum[:, :], scalar=0.5, in1=z[:, m, :],
                                               op0=ALU.mult, op1=ALU.mult).then_inc(y_done, 1)

            def center(name, src, dst, done):
                full(dve, name)
                for k in range(KD):
                    nc.vector.tensor_tensor(dst[:, k, :], src[:, k, :], bank(name), ALU.subtract).then_inc(centered, 1)
                dve.wait_ge(centered, KD * done)
                dve.sem_inc(free_of(name), 1)

            def silu2(s, name, dst):
                i = silus[s]
                dve.wait_ge(th_done, i + 1)
                return nc.vector.scalar_tensor_tensor(out=dst, in0=th[:, i % 2, :], scalar=1.0, in1=bank(name),
                                                      op0=ALU.add, op1=ALU.mult)

            def step(s):
                kind, c = s[0], s[1]
                if kind == "scan":
                    scan(s[1])
                elif kind == "times_c":
                    times_c(s[1])
                elif kind == "add_states":
                    add_states(s[1])
                elif kind == "gate":
                    gate_y(s[1])
                elif kind == "split_low":
                    split_low(s[1])
                elif kind == "ln1_mean":
                    center(s, h[:, c, :, :], a[:, c, :, :], ln_index("ln1", c) + 1)
                elif kind == "ln2_mean":
                    dve.wait_ge(h1_done, KD * (c + 1))
                    center(s, h[:, c, :, :], a[:, c, :, :], ln_index("ln2", c) + 1)
                elif kind in ("ln1_var", "ln2_var"):
                    name = kind[0:3]
                    dst = a[:, c, :, :] if name == "ln1" else sq[:, :, :]
                    dve.wait_ge(rstd_done, norm_index(name, c) + 1)
                    for k in range(KD):
                        nc.vector.tensor_tensor(dst[:, k, :], a[:, c, k, :], rstd[:, :], ALU.mult).then_inc(norm_done, 1)
                    if name == "ln2":
                        hn2_low(c, 1)
                elif kind in ("rms1", "rms2"):
                    dve.wait_ge(rstd_done, norm_index(kind, c) + 1)
                    if (kind, c) == ("rms1", 1):
                        full(dve, ("in_z", 0, KI - 1))
                    dst, w = (hn, S_W1) if kind == "rms1" else (sq, S_W2)
                    for k in range(KD):
                        nc.vector.scalar_tensor_tensor(out=dst[:, k, :], in0=a[:, c, k, :], scalar=small_ap(w, k),
                                                       in1=rstd[:, :], op0=ALU.mult, op1=ALU.mult).then_inc(norm_done, 1)
                    if kind == "rms2":
                        hn2_low(c, 0)
                elif kind == "in_c":
                    t = KI * c + s[2]
                    dve.wait_ge(c_hi_done, t + 1)
                    nc.vector.tensor_tensor(c_part[:, 1, :], bank(s), c_part[:, 0, :].bitcast(F32),
                                            ALU.subtract).then_inc(c_lo_done, 1)
                    dve.wait_ge(c_lo_done, t + 1)
                    dve.sem_inc(free_of(s), 1)
                elif kind == "in_z":
                    if c >= 1:
                        dve.wait_ge(y_done, KI * (c - 1) + s[2] + 1)
                    silu2(s, s, z[:, s[2], :]).then_inc(z_ready, 1)
                    dve.wait_ge(z_ready, KI * c + s[2] + 1)
                    dve.sem_inc(free_of(s), 1)
                    dve.sem_inc(th_used, 1)
                elif kind == "dtp":
                    i = KI * c + s[2]
                    dve.wait_ge(sp_act, 2 * i + 2)
                    link(nc.vector.tensor_scalar(sp_e[:, :], sp_u[:, :], 1.0, -1.0, ALU.add, ALU.add))
                    nc.vector.tensor_tensor(sp_u[:, :], sp_u[:, :], sp_e[:, :], ALU.subtract).then_inc(sp_rest, 1)
                elif kind == "out":
                    full(dve, s)
                    nc.vector.tensor_tensor(a[:, c, s[2], :], a[:, c, s[2], :], bank(s), ALU.add).then_inc(res_done, 1)
                    dve.wait_ge(res_done, KD * c + s[2] + 1)
                    dve.sem_inc(free_of(s), 1)
                elif kind == "gu":
                    n, j = tile_of(s), s[4]
                    if n == 0:
                        dve.wait_ge(dt_ready, NCH * KI)
                    link(silu2(s, (s, "gate"), gate2[:, :]))
                    dve.sem_inc(free_of((s, "gate")), 1)
                    dve.sem_inc(th_used, 1)
                    full(dve, s)
                    if n >= 2:
                        dve.wait_ge(gated_lo, n - 1)
                    nc.vector.scalar_tensor_tensor(out=gated_f[:, n % 2, :], in0=gate2[:, :], scalar=0.5, in1=bank((s, "up")),
                                                   op0=ALU.mult, op1=ALU.mult).then_inc(gated_raw, 1)
                    if j >= 1:
                        gated_low(n - 1)
                    dve.wait_ge(gated_raw, n + 1)
                    dve.sem_inc(free_of((s, "up")), 1)
                    if j == HH - 1:
                        gated_low(n)
                elif kind == "down":
                    mlp, half, o = s[2], s[3], s[4]
                    full(dve, s)
                    into = a if mlp == 0 else h
                    ins = nc.vector.tensor_tensor(into[:, c, o, :], into[:, c, o, :], bank(s), ALU.add)
                    if (mlp, half) == (1, 1):
                        ins.then_inc(final_done, 1)
                        dve.wait_ge(final_done, KD * c + o + 1)
                    else:
                        link(ins)
                    dve.sem_inc(free_of(s), 1)
                    if (mlp, half) == (0, 1):
                        nc.vector.tensor_tensor(h[:, c, o, :], h[:, c, o, :], a[:, c, o, :], ALU.add).then_inc(h1_done, 1)

            def split_low(k):
                dve.wait_ge(w_hi_done, k + 1)
                nc.vector.tensor_tensor(ws[:, k % NW, 1, :], wraw[:, split_loads[k] % NRAW, :],
                                        ws[:, k % NW, 0, :].bitcast(F32), ALU.subtract).then_inc(w_lo_dve, 1)

            def gated_low(n):
                dve.wait_ge(gated_hi, n + 1)
                nc.vector.tensor_tensor(gated[:, 1, n % HH, :], gated_f[:, n % 2, :], gated[:, 0, n % HH, :].bitcast(F32),
                                        ALU.subtract).then_inc(gated_lo, 1)

            def hn2_low(c, mlp):
                n = mlp_norm(c, mlp)
                for k in range(KD):
                    dve.wait_ge(hn2_hi, KD * n + k + 1)
                    nc.vector.tensor_tensor(hn2[:, 1, k, :], sq[:, k, :], hn2[:, 0, k, :].bitcast(F32),
                                            ALU.subtract).then_inc(hn2_lo, 1)

            for unit, steps in late(slots, 1):
                parts = []
                if unit is not None:
                    parts = [("scan", unit), ("times_c", unit), ("add_states", unit)]
                    if unit % QU == 0 and 0 < unit <= UNITS:
                        parts.append(("gate", unit // QU - 1))
                    elif unit % QU == 0 and unit > UNITS:
                        parts.insert(2, ("gate", unit // QU - 1))
                    if unit == NCH * UNITS - 1:
                        parts.append(("gate", NCH * KI - 1))
                others = []
                for s in steps:
                    others += [s] + [("split_low", k) for k in splits_at(s) if on_dve(k)]
                if unit is not None and unit >= MIXED_FROM:
                    order = [x for i, p in enumerate(parts) for x in [p] + others[i:i + 1]] + others[len(parts):]
                else:
                    order = parts + others
                for s in order:
                    step(s)

        @block.tensor
        def _(pe):
            def product(name, pairs):
                b, n = uses[name]
                if n >= 1:
                    pe.wait_ge(bank_free[b], n)
                elif b == NG - 1:
                    pe.wait_ge(sum_read, KI)
                for k, (w, x, *ready) in enumerate(pairs):
                    if ready:
                        pe.wait_ge(*ready)
                    last = nc.tensor.matmul(work[b][:, 0:T], w, x, start=(k == 0), stop=(k == len(pairs) - 1))
                last.then_inc(bank_full[b], 1)

            def c_broadcast(u):
                c, m, q = u // UNITS, u % UNITS // QU, u % QU
                t = KI * c + m
                if u == 0:
                    pe.wait_ge(pick_done, 1)
                pe.wait_ge(c_loaded[t % NC], 64 * (t // NC + 1))
                for half in range(2):
                    if u >= 1:
                        pe.wait_ge(c_free, 2 * (u - 1) + half + 1)
                    for i in range(2):
                        lo = (2 * half + i) * P
                        rows = slice(64 * (q % 2), 64 * (q % 2) + 64)
                        last = nc.tensor.matmul(cps[half][:, i, 0:T], pick_c[rows, lo:lo + P],
                                                c_st[rows, t % NC, q // 2, :], start=True, stop=True)
                    last.then_inc(c_full, 1)

            def state_sum(u):
                m, q = u // QU, u % QU
                if q == 0 and m >= 1:
                    pe.wait_ge(sum_read, m)
                if q in HALVED:
                    pe.wait_ge(halved_done, len(HALVED) * m + HALVED.index(q) + 1)
                else:
                    pe.wait_ge(c_free, 2 * u + 2)
                states = NQ // 2 if q in HALVED else NQ
                for i in range(states):
                    last = nc.tensor.matmul(work[NG - 1][:, 0:T], sm[:, S_IDENT:S_IDENT + P], hs[:, u % NH, i, :],
                                            start=(q == 0 and i == 0), stop=(q == QU - 1 and i == states - 1))
                    if i < states - 1:
                        continue
                    last.then_inc(h_summed, 1)
                if q == QU - 1:
                    pe.wait_ge(h_summed, u + 1)
                    pe.sem_inc(sum_done, 1)

            def split_products(w, x, *ready):
                return [(w[i], x[j], *ready) for i, j in ((0, 0), (0, 1), (1, 0))]

            def split_weights(s, i):
                return [ws[:, split_of[s] % NW, part, i * P:(i + 1) * P] for part in range(2)]

            def keep_clock():
                for _ in range(KEEP_CLOCK):
                    nc.tensor.matmul(cps[0][:, 0, 0:P], mean_w[:, :], mean_w[:, :], start=True, stop=True)

            def step(s):
                kind, c = s[0], s[1]
                if kind == "tok":
                    if c == 0:
                        pe.wait_ge(pat_loaded, 16)
                        pe.wait_ge(tokw_loaded, 16)
                    for k in range(KD):
                        product(("tok", c, k), [(tokw[:, k * P:(k + 1) * P], pat[:, c, :])])
                elif kind in ("ln1_mean", "ln2_mean"):
                    if kind == "ln1_mean":
                        pe.wait_ge(consts_done, 1)
                    written = h_done if kind == "ln1_mean" else h1_done
                    product(s, [(mean_w[:, :], h[:, c, k, :], written, KD * c + k + 1) for k in range(KD)])
                elif kind in ("ln1_var", "ln2_var", "rms1", "rms2"):
                    v = norm_index(kind[0:3] if kind[0] == "l" else kind, c)
                    product(s, [(mean_w[:, :], sq[:, k, :], sq_done, KD * v + k + 1) for k in range(KD)])
                    if kind in ("rms2", "ln2_var") and c == NCH - 1:
                        pe.wait_ge(c_free, 2 * NCH * UNITS)
                        keep_clock()
                elif kind in ("in_dt", "in_x", "in_b", "in_c", "in_z"):
                    t = {"in_dt": IN_DT, "in_x": IN_X + s[-1], "in_b": IN_B + s[-1], "in_c": IN_CZ + 2 * s[-1],
                         "in_z": IN_CZ + 2 * s[-1] + 1}[kind]
                    v = norm_index("rms1", c)
                    if c == 0:
                        for g, (lo, hi) in enumerate(IN_GROUPS):
                            if lo == t:
                                pe.wait_ge(win_loaded[g], 16)
                    product(s, [(win[:, t, k * P:(k + 1) * P], hn[:, k, :], norm_done, KD * v + k + 1) for k in range(KD)])
                elif kind == "dtp":
                    if c == 0 and s[2] == 0:
                        pe.wait_ge(wdt_loaded, 16)
                    pe.wait_ge(dti_done, c + 1)
                    product(s, [(wdt[:, s[2] * P:(s[2] + 1) * P], dti[:, :])])
                elif kind == "xs":
                    m = s[2]
                    if c == 0 and m == 0:
                        pe.wait_ge(small_loaded, 16)
                    pe.wait_ge(xv_done, 2 * c + m // 4 + 1)
                    rows = slice(32 * (m % 4), 32 * (m % 4) + 32)
                    product(s, [(sm[rows, S_PICKX:S_PICKX + P], xv[rows, m // 4, :])])
                elif kind == "out":
                    i = load_of[s]
                    pe.wait_ge(w_loaded[i % NRAW], 16 * (i // NRAW + 1))
                    product(s, [(wraw[:, i % NRAW, m * P:(m + 1) * P], yg[:, m, :], y_done, KI * c + m + 1)
                                for m in range(KI)])
                elif kind == "gu":
                    n = mlp_norm(c, s[2])
                    low_part(pe, split_of[s])
                    for i, part in enumerate(("gate", "up")):
                        product((s, part), [p for k in range(KD) for p in
                                            split_products(
                                                split_weights(s, KD * i + k), [hn2[:, j, k, :] for j in range(2)],
                                                hn2_lo, KD * n + k + 1)])
                elif kind == "down":
                    done = HH * (4 * c + 2 * s[2] + s[3])
                    low_part(pe, split_of[s])
                    product(s, [p for k in range(HH) for p in
                                split_products(split_weights(s, k), [gated[:, j, k, :] for j in range(2)], gated_lo, done + k + 1)])

            for unit, steps in slots:
                if unit is not None:
                    c_broadcast(unit)
                    if 0 < unit <= UNITS:
                        state_sum(unit - 1)
                for s in steps:
                    step(s)


def kernel(**inputs):
    import numpy as np
    import concourse.bacc as bacc
    from concourse.bass_utils import run_bass_kernel_spmd

    g = {k: np.asarray(v) for k, v in inputs.items()}
    f = np.float32

    def cols(v, n):
        return v.reshape(n, P).T

    x = g["x"][:, :, 0]
    starts = [i * HOP for i in range(STEPS)]
    pat = np.stack([x[:, s:s + PATCH] for s in starts], 1).reshape(BATCH * STEPS, PATCH).T
    pat = pat.reshape(P, NCH, T)

    wi = g["L0_attn_in_proj_w"]
    z0, x0, b0, c0, d0 = 0, DI, DI + XB, DI + 2 * XB, 2 * DI + 2 * XB
    starts = [d0, x0, x0 + P, b0, b0 + P]
    for m in range(KI):
        starts += [c0 + m * P, z0 + m * P]
    by_state = np.arange(P).reshape(P // NS, NS).T.ravel()
    order = {s: (s + by_state if c0 <= s < c0 + DI else s + np.arange(P)) for s in starts}
    w_in = np.stack([wi[order[s]].T.reshape(KD, P, P).transpose(1, 0, 2).reshape(P, D) for s in starts], 1)

    row, ch = np.arange(P)[:, None] % 32, np.arange(P)[None, :]
    pick_x = (row == 16 * (ch // 64) + ch % 16).astype(f)
    pick_c = np.concatenate([row == (P // NS) * i + ch // 16 for i in range(NQ)], 1).astype(f)
    small = np.concatenate([
        cols(g["L0_tok_b"], KD), cols(g["L0_attn_dt_proj_b"], KI), cols(g["L0_attn_D_skip"], KI),
        cols(g["L0_attn_rms1_w"], KD), cols(g["L0_attn_rms2_w"], KD),
        g["L0_attn_A_log"].reshape(KI, P, NS).transpose(1, 0, 2).reshape(P, KI * NS), pick_x, np.eye(P, dtype=f)], 1)

    def mlp(gate, up, down):
        gt = gate.T.reshape(KD, P, HT, P).transpose(2, 1, 0, 3).reshape(HT, P, D)
        ut = up.T.reshape(KD, P, HT, P).transpose(2, 1, 0, 3).reshape(HT, P, D)
        gu = np.concatenate([gt, ut], 2)
        dn = down.reshape(KD, P, 2, HH, P).transpose(2, 0, 4, 3, 1).reshape(2, KD, P, WSLOT)
        return [gu[:HH], dn[0], gu[HH:], dn[1]]

    wo = g["L0_attn_out_proj_w"].reshape(KD, P, KI, P).transpose(0, 3, 2, 1).reshape(KD, P, WSLOT)
    w_stream = np.concatenate([wo] + mlp(g["L0_attn_gate_w"], g["L0_attn_up_w"], g["L0_attn_down_w"])
                           + mlp(g["L0_ffn_w_gate"], g["L0_ffn_w_up"], g["L0_ffn_w_down"]), 0)
    arrays = {
        "patches": pat, "tok_w": g["L0_tok_W"].T, "small": small, "pick": pick_c, "w_in": w_in, "w_dt": g["L0_attn_dt_proj_w"].T,
        "w_stream": w_stream}
    arrays = {k: np.ascontiguousarray(v) for k, v in arrays.items()}

    nc = bacc.Bacc("TRN2", target_bir_lowering=False, num_devices=1)
    aps = [nc.dram_tensor(k, v.shape, mybir.dt.from_np(v.dtype), kind="ExternalInput").ap() for k, v in arrays.items()]
    out = nc.dram_tensor("out", (D, BATCH * STEPS), F32, kind="ExternalOutput").ap()
    build(nc, *aps, out)
    r = run_bass_kernel_spmd(nc, [arrays], core_ids=[0])
    return np.ascontiguousarray(r.results[0]["out"].T).reshape(BATCH, STEPS, D)
```
